# Optimizing a Trainium2 kernel written in Bass

```python
import numpy as np
import jax
import jax.numpy as jnp

def _softmax(x, axis=-1):
    return jax.nn.softmax(x, axis=axis)

def _gelu(x):
    return jax.nn.gelu(x, approximate=True)

def _silu(x):
    return jax.nn.silu(x)

def _sigmoid(x):
    return jax.nn.sigmoid(x)

def _layernorm(x, axis=-1, eps=1e-05):
    m = jnp.mean(x, axis=axis, keepdims=True)
    v = jnp.var(x, axis=axis, keepdims=True)
    return (x - m) / jnp.sqrt(v + eps)

def _scatter_add(tgt, idx, src, axis=0):
    return tgt.at[idx].add(src)

def _segment_sum(src, seg, n):
    return jax.ops.segment_sum(src, seg, n)
kernel_name = 'mk_prb_d2_jaxref_r8_5c0f8c'

def setup_inputs(seed: int=0):
    np.random.seed(seed)
    _w = jnp.asarray

    def _L0_attn_setup():
        import jax, jax.numpy as jnp
        import numpy as np
        B, S, E, H, D = (4, 256, 128, 16, 64)

        def _large_negative_number(dtype):
            return jnp.asarray(-0.7 * jnp.finfo(dtype).max, dtype=dtype)
        key = jax.random.key(seed)
        k1, k2, k3 = jax.random.split(key, 3)
        x = jax.random.normal(k1, (B, S, E), dtype=jnp.float32)
        qkv_w = jax.random.normal(k2, (E, H, 3 * D), dtype=jnp.float32) * (1.0 / np.sqrt(E))
        qkv_b = jnp.zeros((H, 3 * D), dtype=jnp.float32)
        out_w = jax.random.normal(k3, (H, D, E), dtype=jnp.float32) * (1.0 / np.sqrt(H * D))
        out_b = jnp.zeros((E,), dtype=jnp.float32)
        return {'x': x, 'qkv_w': qkv_w, 'qkv_b': qkv_b, 'out_w': out_w, 'out_b': out_b}
    _L0_attn_in = _L0_attn_setup()

    def _L0_ffn_setup():
        import jax, jax.numpy as jnp
        import numpy as np
        B, S, D, H, E = (4, 256, 128, 16, 4)
        key = jax.random.key(seed)
        ks = jax.random.split(key, 8)
        w = lambda k, shape: jax.random.normal(k, shape, jnp.float32) * 0.02
        return {'x': jax.random.normal(ks[0], (B, S, D), jnp.float32), 'router_w': w(ks[1], (D, E)), 'router_b': jnp.zeros((E,), jnp.float32), 'wq': w(ks[2], (E, D, D)), 'bq': jnp.zeros((E, D), jnp.float32), 'wk': w(ks[3], (E, D, D)), 'bk': jnp.zeros((E, D), jnp.float32), 'wv': w(ks[4], (E, D, D)), 'bv': jnp.zeros((E, D), jnp.float32), 'wo': w(ks[5], (E, D, D)), 'bo': jnp.zeros((E, D), jnp.float32)}
    _L0_ffn_in = _L0_ffn_setup()

    def _L1_attn_setup():
        import jax, jax.numpy as jnp
        import numpy as np
        B, N, D = (2, 256, 128)
        H, DH = (16, 64)
        SOFTCLAMP = 50.0
        SCALE = DH ** (-0.5)
        key = jax.random.key(seed)
        ks = jax.random.split(key, 5)
        std = D ** (-0.5)
        return {'x': jax.random.normal(ks[0], (B, N, D), dtype=jnp.float32), 'Wq': jax.random.normal(ks[1], (H * DH, D), dtype=jnp.float32) * std, 'Wk': jax.random.normal(ks[2], (H * DH, D), dtype=jnp.float32) * std, 'Wv': jax.random.normal(ks[3], (H * DH, D), dtype=jnp.float32) * std, 'Wo': jax.random.normal(ks[4], (D, H * DH), dtype=jnp.float32) * std}
    _L1_attn_in = _L1_attn_setup()

    def _L1_ffn_setup():
        import jax, jax.numpy as jnp
        import numpy as np
        B, S, D_MODEL, D_FF = (4, 256, 128, 512)

        def _quantum_transform(hidden, theta, w_real, w_imag):
            imag = w_imag * jnp.sin(theta + hidden * 0.1)
            quantum_phase = jnp.cos(theta) * w_real + jnp.sin(theta) * w_imag
            return hidden + quantum_phase * imag * 0.1
        key = jax.random.key(seed)
        ks = jax.random.split(key, 8)
        return {'x': jax.random.normal(ks[0], (B, S, D_MODEL), dtype=jnp.float32), 'W1': jax.random.normal(ks[1], (D_MODEL, D_FF), dtype=jnp.float32) * (1.0 / np.sqrt(D_MODEL)), 'b1': jnp.zeros((D_FF,), dtype=jnp.float32), 'quantum_phases': jax.random.normal(ks[2], (D_FF,), dtype=jnp.float32) * (2.0 * np.pi), 'quantum_weights_real': jax.random.normal(ks[3], (D_FF,), dtype=jnp.float32) * 0.1, 'quantum_weights_imag': jax.random.normal(ks[4], (D_FF,), dtype=jnp.float32) * 0.1, 'W2': jax.random.normal(ks[5], (D_FF, D_MODEL), dtype=jnp.float32) * (1.0 / np.sqrt(D_FF)), 'b2': jnp.zeros((D_MODEL,), dtype=jnp.float32)}
    _L1_ffn_in = _L1_ffn_setup()
    _d = {'L0_attn_x': _L0_attn_in['x'], 'L0_attn_qkv_w': _L0_attn_in['qkv_w'], 'L0_attn_qkv_b': _L0_attn_in['qkv_b'], 'L0_attn_out_w': _L0_attn_in['out_w'], 'L0_attn_out_b': _L0_attn_in['out_b'], 'L0_ffn_router_w': _L0_ffn_in['router_w'], 'L0_ffn_router_b': _L0_ffn_in['router_b'], 'L0_ffn_wq': _L0_ffn_in['wq'], 'L0_ffn_bq': _L0_ffn_in['bq'], 'L0_ffn_wk': _L0_ffn_in['wk'], 'L0_ffn_bk': _L0_ffn_in['bk'], 'L0_ffn_wv': _L0_ffn_in['wv'], 'L0_ffn_bv': _L0_ffn_in['bv'], 'L0_ffn_wo': _L0_ffn_in['wo'], 'L0_ffn_bo': _L0_ffn_in['bo'], 'L1_attn_Wq': _L1_attn_in['Wq'], 'L1_attn_Wk': _L1_attn_in['Wk'], 'L1_attn_Wv': _L1_attn_in['Wv'], 'L1_attn_Wo': _L1_attn_in['Wo'], 'L1_ffn_W1': _L1_ffn_in['W1'], 'L1_ffn_b1': _L1_ffn_in['b1'], 'L1_ffn_quantum_phases': _L1_ffn_in['quantum_phases'], 'L1_ffn_quantum_weights_real': _L1_ffn_in['quantum_weights_real'], 'L1_ffn_quantum_weights_imag': _L1_ffn_in['quantum_weights_imag'], 'L1_ffn_W2': _L1_ffn_in['W2'], 'L1_ffn_b2': _L1_ffn_in['b2']}
    _x0 = _d['L0_attn_x']
    _d['L0_attn_x'] = jax.random.normal(jax.random.fold_in(jax.random.key(seed), 1), (16, 256, 128), dtype=_x0.dtype)
    del _x0
    return _d

def reference(L0_attn_x, L0_attn_qkv_w, L0_attn_qkv_b, L0_attn_out_w, L0_attn_out_b, L0_ffn_router_w, L0_ffn_router_b, L0_ffn_wq, L0_ffn_bq, L0_ffn_wk, L0_ffn_bk, L0_ffn_wv, L0_ffn_bv, L0_ffn_wo, L0_ffn_bo, L1_attn_Wq, L1_attn_Wk, L1_attn_Wv, L1_attn_Wo, L1_ffn_W1, L1_ffn_b1, L1_ffn_quantum_phases, L1_ffn_quantum_weights_real, L1_ffn_quantum_weights_imag, L1_ffn_W2, L1_ffn_b2):

    def _L0_attn_ref(x, qkv_w, qkv_b, out_w, out_b):
        import jax, jax.numpy as jnp
        import numpy as np
        B, S, E, H, D = (4, 256, 128, 16, 64)

        def _large_negative_number(dtype):
            return jnp.asarray(-0.7 * jnp.finfo(dtype).max, dtype=dtype)
        qkv = jnp.einsum('bse,ehd->bshd', x, qkv_w) + qkv_b
        q, k, v = jnp.split(qkv, 3, axis=-1)
        logits = jnp.einsum('bqhd,bkhd->bhqk', q, k)
        logits = logits / jnp.sqrt(jnp.asarray(q.shape[-1], logits.dtype))
        mask = jnp.tril(jnp.ones((q.shape[1], q.shape[1]), dtype=jnp.bool_))
        logits = jnp.where(mask, logits, _large_negative_number(logits.dtype))
        probs = jax.nn.softmax(logits, axis=-1)
        attn = jnp.einsum('bhqk,bkhd->bqhd', probs, v)
        return jnp.einsum('bqhd,hde->bqe', attn, out_w) + out_b

    def _L0_ffn_ref(x, router_w, router_b, wq, bq, wk, bk, wv, bv, wo, bo):
        import jax, jax.numpy as jnp
        import numpy as np
        B, S, D, H, E = (4, 256, 128, 16, 4)
        b, s, d = x.shape
        e_total = router_w.shape[-1]
        h = H
        hd = d // h
        sm_scale = 0.5
        logits = x @ router_w + router_b
        probs = jax.nn.softmax(logits, axis=-1)
        _, top2 = jax.lax.top_k(probs, 2)
        out = jnp.zeros_like(x)
        bidx = jnp.arange(b)[:, None]
        for e in range(e_total):
            member = (top2 == e).any(-1)
            w_tok = jnp.where(member, probs[..., e], 0.0)
            order = jnp.argsort((~member).astype(jnp.int32), axis=-1, stable=True)
            xg = jnp.take_along_axis(x, order[..., None], axis=1)
            validg = jnp.take_along_axis(member, order, axis=1)
            wg = jnp.take_along_axis(w_tok, order, axis=1)
            q = (xg @ wq[e] + bq[e]).reshape(b, s, h, hd)
            k = (xg @ wk[e] + bk[e]).reshape(b, s, h, hd)
            v = (xg @ wv[e] + bv[e]).reshape(b, s, h, hd)
            att = jnp.einsum('bqhd,bkhd->bhqk', q, k) * sm_scale
            att = jnp.where(validg[:, None, None, :], att, -1000000000.0)
            att = jax.nn.softmax(att, axis=-1)
            y = jnp.einsum('bhqk,bkhd->bqhd', att, v).reshape(b, s, d)
            y = y @ wo[e] + bo[e]
            out = out.at[bidx, order].add(wg[..., None] * y)
        return out

    def _L1_attn_ref(x, Wq, Wk, Wv, Wo):
        import jax, jax.numpy as jnp
        import numpy as np
        B, N, D = (2, 256, 128)
        H, DH = (16, 64)
        SOFTCLAMP = 50.0
        SCALE = DH ** (-0.5)
        b, n, _ = x.shape
        q = jnp.einsum('bnd,fd->bnf', x, Wq).reshape(b, n, H, DH).transpose(0, 2, 1, 3)
        k = jnp.einsum('bnd,fd->bnf', x, Wk).reshape(b, n, H, DH).transpose(0, 2, 1, 3)
        v = jnp.einsum('bnd,fd->bnf', x, Wv).reshape(b, n, H, DH).transpose(0, 2, 1, 3)
        sim = jnp.einsum('bhid,bhjd->bhij', q, k) * SCALE
        sim = SOFTCLAMP * jnp.tanh(sim / SOFTCLAMP)
        causal = jnp.tril(jnp.ones((n, n), dtype=bool))
        sim = jnp.where(causal, sim, jnp.finfo(sim.dtype).min)
        attn = jax.nn.softmax(sim, axis=-1)
        out = jnp.einsum('bhij,bhjd->bhid', attn, v)
        out = out.transpose(0, 2, 1, 3).reshape(b, n, H * DH)
        return jnp.einsum('bnf,df->bnd', out, Wo)

    def _L1_ffn_ref(x, W1, b1, quantum_phases, quantum_weights_real, quantum_weights_imag, W2, b2):
        import jax, jax.numpy as jnp
        import numpy as np
        B, S, D_MODEL, D_FF = (4, 256, 128, 512)

        def _quantum_transform(hidden, theta, w_real, w_imag):
            imag = w_imag * jnp.sin(theta + hidden * 0.1)
            quantum_phase = jnp.cos(theta) * w_real + jnp.sin(theta) * w_imag
            return hidden + quantum_phase * imag * 0.1
        hidden = jnp.einsum('bsd,df->bsf', x, W1) + b1
        q = _quantum_transform(hidden, quantum_phases, quantum_weights_real, quantum_weights_imag)
        act = jax.nn.relu(q)
        return jnp.einsum('bsf,fd->bsd', act, W2) + b2
    x = L0_attn_x
    xn = _layernorm(x, axis=-1)
    x = x + _L0_attn_ref(xn, L0_attn_qkv_w, L0_attn_qkv_b, L0_attn_out_w, L0_attn_out_b) + _L0_ffn_ref(xn, L0_ffn_router_w, L0_ffn_router_b, L0_ffn_wq, L0_ffn_bq, L0_ffn_wk, L0_ffn_bk, L0_ffn_wv, L0_ffn_bv, L0_ffn_wo, L0_ffn_bo)
    xn = _layernorm(x, axis=-1)
    x = x + _L1_attn_ref(xn, L1_attn_Wq, L1_attn_Wk, L1_attn_Wv, L1_attn_Wo) + _L1_ffn_ref(xn, L1_ffn_W1, L1_ffn_b1, L1_ffn_quantum_phases, L1_ffn_quantum_weights_real, L1_ffn_quantum_weights_imag, L1_ffn_W2, L1_ffn_b2)
    return x

_drawn_inputs = setup_inputs


def setup_inputs(seed=0):
    import zlib

    import numpy as np

    out = dict(_drawn_inputs(seed))
    spreads = {'L0_attn_qkv_b': (0.0, 0.1),
     'L0_attn_out_b': (0.0, 0.1),
     'L0_ffn_router_b': (0.0, 0.56),
     'L0_ffn_bq': (0.0, 0.8),
     'L0_ffn_bk': (0.0, 2.0),
     'L0_ffn_bv': (0.0, 0.566),
     'L0_ffn_bo': (0.0, 0.1),
     'L1_ffn_b1': (0.0, 0.1),
     'L1_ffn_b2': (0.0, 0.1)}
    factors = {'L0_ffn_wq': 8.0,
     'L0_ffn_wk': 8.0,
     'L0_ffn_wv': 8.0,
     'L0_ffn_wo': 3.598,
     'L1_ffn_quantum_phases': 22.639,
     'L1_ffn_quantum_weights_real': 45.296,
     'L1_ffn_quantum_weights_imag': 8.0}
    for name, (base, spread) in spreads.items():
        noise = np.random.default_rng([zlib.crc32(name.encode()), seed]).standard_normal(out[name].shape)
        drawn = base * np.exp(spread * noise) if base else spread * noise
        out[name] = jnp.asarray(drawn.astype(out[name].dtype))
    for name, factor in factors.items():
        out[name] = (out[name] * factor).astype(out[name].dtype)
    return out
```

```python
from contextlib import ExitStack

import concourse.bass as bass
from concourse import mybir

F32 = mybir.dt.float32
F32R = mybir.dt.float32r
ACT = mybir.ActivationFunctionType
ALU = mybir.AluOpType
AX = mybir.AxisListType

BATCH, SEQ, D = 16, 256, 128
P = 128
BLKS = SEQ // P
HEADS, DH = 16, 64
PAIRS = HEADS // 2
EXPERTS, HE = 4, 8
GROUPS, GH = 4, 4
SLOTS = 2 * SEQ
FF = 512
FBLK = FF // P
EPS = 1e-5
L0_SCALE = DH ** -0.5
ROUTED_SCALE = 0.5
CLAMP = 50.0
FAR = 1e30
PI = 3.141592653589793
MAGIC = 1.5 * 2.0 ** 23
TWO_PI_PARTS = (6.28125, 0.0019350051879882812, 3.0199157663446385e-07)
DHV = DH + 1
QAUX = 96
RMAXROW = QAUX + EXPERTS
AUXC = 12

CONST = {}
_at = 0
for _name, _width in (("ident", P), ("spread", GROUPS * P), ("expand", 2 * P),
                      ("sumcols", GROUPS * 32), ("tie", BLKS * 16), ("pick", GH * P), ("negident", P)):
    CONST[_name] = (_at, _width)
    _at += _width
CONST_W = _at
CONST_KEPT = CONST["pick"][0]


class Uses:

    def __init__(self, keys_and_banks):
        self.n, self.where = {}, {}
        for key, bank in keys_and_banks:
            self.where[key] = (bank, self.n.get(bank, 0))
            self.n[bank] = self.n.get(bank, 0) + 1

    def bank(self, key):
        return self.where[key][0]

    def before(self, j, key):
        bank, k = self.where[key]
        return j * self.n[bank] + k

    def after(self, j, key):
        bank, k = self.where[key]
        return j * self.n[bank] + (k + 1)


def pe_order():
    s = [("T0",), ("RL",), ("Ap", 0), ("Ap", 1)]
    s += [("Av", i) for i in range(4)]
    s += [("Am", 0), ("Am", 1), ("Ap", 2), ("Ap", 3), ("RT",), ("SB",), ("WB",)]
    for g in range(4):
        s += [("An", g)]
        if g < 3:
            s += [("Am", 2 * g + 2), ("Am", 2 * g + 3)]
        s += [("As", 2 * g), ("As", 2 * g + 1)]
        if g < 2:
            s += [("Ap", 2 * g + 4), ("Ap", 2 * g + 5)]
        if g == 2:
            s += [("Fp", 0)]
        if g == 3:
            s += [("Fp", 1)]
        s += [("Ao", 2 * g), ("Ao", 2 * g + 1)]
    s += [("Fv", 0), ("Fv", 1), ("Fp", 2)]
    s += [("At", m) for m in range(4)]
    s += [("Fm", 0, h) for h in range(GH)]
    for g in range(4):
        s += [("Fn", g)]
        if g < 3:
            s += [("Fm", g + 1, h) for h in range(GH)]
        s += [("Fs", g, 0), ("Fs", g, 1), ("Fs", g, 2), ("Fo", g, 0), ("Fs", g, 3), ("Fo", g, 1)]
        if g == 1:
            s += [("Fp", 3)]
    s += [("Fe", g) for g in range(4)]
    s += [("X1",), ("T1",), ("Cp", 0), ("Cp", 1)]
    s += [("Cs", 0)]
    s += [("Cv", i) for i in range(4)]
    for p in range(8):
        if p < 6:
            s += [("Cp", p + 2)]
        if p < 7:
            s += [("Cs", p + 1)]
        s += [("Co", p)]
    s += [("Ct", m) for m in range(4)]
    s += [("X2",)]
    return s


ORDER = pe_order()
PROJ_STEPS = {"T0", "RL", "Ap", "Av", "RT", "SB", "WB", "An", "Fp", "Fv", "At", "Fn", "Fe", "X1", "T1",
              "Cp", "Cv", "Ct", "X2"}


def alternate(steps, first):
    return [(key, first + i % 2) for i, key in enumerate(steps)]


PROJ = Uses(alternate([s for s in ORDER if s[0] in PROJ_STEPS], 0))
SCORES = Uses(alternate([s for s in ORDER if s[0] in ("Am", "As", "Fm", "Fs", "Cs")], 0))
OUTS = Uses([(s, s[1] % 2) if s[0] in ("Ao", "Co") else (("Fo", s[1]), 0)
             for s in ORDER if s[0] in ("Ao", "Co") or (s[0] == "Fo" and s[2] == 0)] )
OUTS.where[("Fsum",)] = (1, 4)
for _p in (1, 3, 5, 7):
    OUTS.where[("Co", _p)] = (1, 5 + _p // 2)
OUTS.n[1] += 1
PROBS = Uses([(s, i % 4) for i, s in enumerate([s for s in ORDER if s[0] in ("As", "Fs", "Cs")])])


def exp_order():
    return [s for s in ORDER if s[0] in ("As", "Fs", "Cs")]


EXPS = {s: i for i, s in enumerate(exp_order())}
NEXP = len(EXPS)
MASKED = {s: i for i, s in enumerate([s for s in exp_order() if s[0] in ("As", "Cs")])}
NMASK = len(MASKED)
SCRATCH_W = 4096


def blocks(nc, x, w_l0, w_l1, w_ffn, w_ff1, router_w, out_w0, out_w1, wo, w_ff2, bias_qk0, bias_v0, bias_qkf,
           bias_vf, router_b, out_b, bo, ff_cols, ff_b2, consts, scratch_x, scratch_t, out):
    with ExitStack() as ctx:
        def sb(name, shape, dt=F32):
            return ctx.enter_context(nc.sbuf_tensor(name, shape, dt))

        def sem(name):
            return ctx.enter_context(nc.semaphore(name))

        ps = ctx.enter_context(nc.psum_tensor("ps", [P, 8, 512], F32))

        W = {}
        for name, n in (("l0", 3072), ("l1", 3072), ("ffn", 1536), ("rt", EXPERTS)):
            W[name] = (sb(f"w_{name}_hi", [P, n], F32R), sb(f"w_{name}_lo", [P, n], F32R))
        w_out = [sb("w_out0", [P, 8, P]), sb("w_out1", [P, 8, P])]
        w_o = sb("w_o", [P, GROUPS, P])
        w_2 = sb("w_2", [P, FBLK, P])
        b_qk0 = sb("b_qk0", [P, 16])
        b_v0 = sb("b_v0", [P, HEADS, DH])
        b_qkf = sb("b_qkf", [P, 8])
        b_vf = sb("b_vf", [P, 512])
        b_rt = sb("b_rt", [P, BLKS * EXPERTS])
        b_out = sb("b_out", [P, P])
        b_o = sb("b_o", [AUXC, P])
        b_2 = sb("b_2", [P, P])
        fc = sb("fc", [P, 4, FBLK])
        cst = sb("cst", [P, CONST_KEPT])
        negident = sb("negident_r", [P, P], F32R)
        pick = sb("pick_r", [GH, GH, P], F32R)

        xin = sb("xin", [P, BLKS, D])
        xres = sb("xres", [P, BLKS, D])
        xn = sb("xn", [P, BLKS, D])
        xt_hi_both, xt_lo_both = sb("xt_hi", [P, 2, SEQ], F32R), sb("xt_lo", [P, 2, SEQ], F32R)
        xt_hi = [xt_hi_both[:, i, :] for i in range(2)]
        xt_lo = [xt_lo_both[:, i, :] for i in range(2)]
        x1 = sb("x1", [P, BLKS, D])
        x2 = sb("x2", [P, BLKS, D])
        st = sb("st", [P, BLKS, 6])
        mv = sb("mv", [P, BLKS, 2])
        rstd, ve, neghalf = sb("rstd", [P, BLKS]), sb("ve", [P, BLKS]), sb("neghalf", [P, BLKS])
        lg = sb("lg", [P, BLKS, EXPERTS])
        ex = sb("ex", [P, BLKS, EXPERTS])
        pr = sb("pr", [P, BLKS, EXPERTS])
        r1 = sb("r1", [P, BLKS])
        r2 = sb("r2", [P, BLKS])
        r3 = sb("r3", [P, BLKS])
        cmp1 = sb("cmp1", [P, BLKS, EXPERTS, EXPERTS])
        cmp2 = sb("cmp2", [P, BLKS, EXPERTS, EXPERTS])
        rank = sb("rank", [P, BLKS, EXPERTS])
        routes = sb("routes", [P, 2, BLKS, AUXC])
        rows = sb("rows", [AUXC, SLOTS])
        rows_r = sb("rows_r", [AUXC, SLOTS], F32R)
        sel_bc = sb("sel_bc", [P, 2, SEQ])
        w_bc = sb("w_bc", [P, SLOTS])
        q_hi = sb("q_hi", [P, 2, SEQ], F32R)
        q_lo = sb("q_lo", [P, 2, SEQ], F32R)
        qs_hi = sb("qs_hi", [P, 2, SEQ], F32R)
        qs_lo = sb("qs_lo", [P, 2, SEQ], F32R)
        RING = 2
        qstack = sb("qstack", [P, RING, GH, SLOTS], F32R)
        kstack = sb("kstack", [P, RING, GH, SEQ], F32R)
        vf = sb("vf", [P, BLKS, 512])
        rmax = sb("rmax", [P, SLOTS // P, HEADS], F32R)
        nmax_f = sb("nmax_f", [GH, SLOTS], F32R)
        rsum = w_bc
        NQK = 4
        qk_hi = sb("qk_hi", [P, NQK, 2, SEQ], F32R)
        qk_lo = sb("qk_lo", [P, NQK, 2, SEQ], F32R)
        v0 = sb("v0", [P, BLKS, HEADS, DHV])
        amax = sb("amax", [P, BLKS, HEADS], F32R)
        nmax_a = sb("nmax_a", [GH, SEQ], F32R)
        ra = sb("ra", [P, 2, 4])
        work = sb("work", [P, 10240])
        probs = work[:, 0:4096].rearrange("p (n c) -> p n c", n=4)
        u = work[:, 4096:6144].rearrange("p (g c) -> p g c", g=GROUPS)
        an = work[:, 6144:8192].rearrange("p (b c) -> p b c", b=BLKS)
        at = work[:, 8192:10240].rearrange("p (m c) -> p m c", m=8)
        y = work[:, 6144:7168].rearrange("p (g c) -> p g c", g=GROUPS)
        y2 = work[:, 7168:8192].rearrange("p (n c s) -> p n c s", n=2, c=2)
        raw, _a = {}, 0
        for name, n in (("l0", 3072), ("l1", 3072), ("ffn", 1536), ("rt", EXPERTS), ("cst", CONST_W - CONST_KEPT)):
            raw[name] = work[:, _a:_a + n]
            _a += n
        act_t = work[:, 0:2048].rearrange("p (f c) -> p f c", f=FBLK)
        turns, whole, frac, sine, pre = (work[:, 2048 + 1024 * i:3072 + 1024 * i].rearrange("p (n c) -> p n c", n=2)
                                         for i in range(5))
        xm_res, xm_resb, xm_out = (work[:, 7168 + 512 * i:7680 + 512 * i].rearrange("p (n c) -> p n c", n=4)
                                   for i in range(3))
        raw["ff1"] = work[:, 8704:8704 + FF]
        W["ff1"] = (q_hi[:].rearrange("p a b -> p (a b)"), q_lo[:].rearrange("p a b -> p (a b)"))
        xm_hi, xm_lo = xt_hi_both, xt_lo_both
        tmp, th, sc_th = (x2[:, 0, 16 * i:16 * i + 16].rearrange("p (n f) -> p n f", f=FBLK) for i in range(3))
        amp = sb("amp", [P, 2, FBLK])

        def const(name):
            a, n = CONST[name]
            return cst[:, a:a + n]

        ident = const("ident")

        proj_full, proj_free = [sem(f"proj_full{i}") for i in (0, 1)], [sem(f"proj_free{i}") for i in (0, 1)]
        sc_full, sc_free = [sem(f"sc_full{i}") for i in (0, 1)], [sem(f"sc_free{i}") for i in (0, 1)]
        out_full, out_free = [sem(f"out_full{i}") for i in (0, 1)], [sem(f"out_free{i}") for i in (0, 1)]
        probs_used = [sem(f"probs_used{i}") for i in range(4)]
        loaded, consts_r, w_hi, w_lo, ones_set = sem("loaded"), sem("consts_r"), sem("w_hi"), sem("w_lo"), sem("ones_set")
        x_in, x_copied, xn_ready = sem("x_in"), sem("x_copied"), sem("xn_ready")
        xt_hi_s, xt_ready = sem("xt_hi_s"), sem("xt_ready")
        waited, dve_c, pool_c, var_ready, rstd_ready = sem("waited"), sem("dve_c"), sem("pool_c"), sem("var_ready"), sem("rstd_ready")
        lg_ready, ex_ready, routes_ready = sem("lg_ready"), sem("ex_ready"), sem("routes_ready")
        rows_ready, rows_r_ready, sel_ready, wbc_ready = sem("rows_ready"), sem("rows_r_ready"), sem("sel_ready"), sem("wbc_ready")
        rows_dma = sem("rows_dma")
        a_hi, a_ready, av_ready = sem("a_hi"), sem("a_ready"), sem("av_ready")
        amax_ready, nmax_a_ready = sem("amax_ready"), sem("nmax_a_ready")
        exp_done, mask_done = sem("exp_done"), sem("mask_done")
        an_ready, at_ready = sem("an_ready"), sem("at_ready")
        f_hi, qs_ready = sem("f_hi"), sem("qs_ready")
        stack_dma = [sem(f"stack_dma{i}") for i in range(RING)]
        rmax_ready, nmax_f_ready, nmax_dma = sem("rmax_ready"), sem("nmax_f_ready"), sem("nmax_dma")
        u_ready, rsum_ready, y2_ready, y_ready = sem("u_ready"), sem("rsum_ready"), sem("y2_ready"), sem("y_ready")
        c_exp, th_ready, sc_ready, amp_c, amp_ready = (sem(n) for n in ("c_exp", "th_ready", "sc_ready", "amp_c",
                                                                        "amp_ready"))
        m_in, m_xin, m_hid, m_turns, m_whole, m_frac, m_sine, m_pre, m_act, m_sum, m_x2, m_out, out_dma = (
            sem(n) for n in ("m_in", "m_xin", "m_hid", "m_turns", "m_whole", "m_frac", "m_sine", "m_pre", "m_act",
                             "m_sum", "m_x2", "m_out", "out_dma"))
        x1_ready, x2_ready = sem("x1_ready"), sem("x2_ready")
        xt1_dma, x2_dma = sem("xt1_dma"), sem("x2_dma")

        def proj(key):
            return ps[:, PROJ.bank(key), :]

        def scores(key):
            b = 2 + 2 * SCORES.bank(key)
            return ps[:, b:b + 2, :]

        def outs(key):
            return ps[:, 6 + OUTS.bank(key), :]

        def full(eng, j, key):
            for uses, sems in ((PROJ, proj_full), (SCORES, sc_full), (OUTS, out_full)):
                if key in uses.where:
                    eng.wait_ge(sems[uses.bank(key)], uses.after(j, key))

        def read(eng, j, key):
            for uses, sems in ((PROJ, proj_free), (SCORES, sc_free), (OUTS, out_free)):
                if key in uses.where:
                    eng.wait_ge(sems[uses.bank(key)], uses.after(j, key))

        def stacked(eng, j, g):
            per = GROUPS // RING
            eng.wait_ge(stack_dma[g % RING], 16 * STACK_DMAS * (per * j + (g // RING + 1)))

        def alone(eng):
            eng.sem_inc(waited, 1)

        def freed(key):
            for uses, sems in ((PROJ, proj_free), (SCORES, sc_free), (OUTS, out_free)):
                if key in uses.where:
                    return sems[uses.bank(key)]

        STACK_DMAS = 26
        SPLIT = ("rt", "l0", "ffn", "l1")
        NLOAD = 19

        scratch_t2 = scratch_t.rearrange("(t b) i p c -> t i b p c", b=2)
        scratch_x2 = scratch_x.rearrange("(t b) k p d -> t (b k) p d", b=2)
        out2 = out.rearrange("(t b) k p d -> t (b k) p d", b=2)

        block = ctx.enter_context(nc.Block())

        RTOT = GROUPS * STACK_DMAS

        @block.sync
        def _(sp):
            for dst, src in ((raw["rt"], router_w), (raw["l0"], w_l0), (raw["ffn"], w_ffn), (raw["l1"], w_l1),
                             (cst[:], consts[:, 0:CONST_KEPT]), (raw["cst"], consts[:, CONST_KEPT:CONST_W]), (b_qk0[:], bias_qk0),
                             (b_v0[:].rearrange("p h d -> p (h d)"), bias_v0),
                             (b_qkf[:], bias_qkf), (b_vf[:], bias_vf), (b_rt[:], router_b), (b_out[:], out_b),
                             (b_o[:], bo), (fc[:], ff_cols), (b_2[:], ff_b2), (w_out[0][:], out_w0),
                             (w_out[1][:], out_w1), (w_o[:], wo), (w_2[:], w_ff2)):
                sp.dma_start(dst, src).then_inc(loaded, 16)
            sp.wait_ge(ones_set, 1)

            def stack(j, g):
                slot = g % RING
                if g >= RING:
                    full(sp, j, ("Fs", g - RING, GH - 1))
                sp.dma_start(qstack[QAUX:QAUX + EXPERTS, slot, :, :].bitcast(F32),
                             rows_r[0:EXPERTS, :].bitcast(F32).rearrange("p (o c) -> p o c", o=1)
                             .to_broadcast([EXPERTS, GH, SLOTS])).then_inc(stack_dma[slot], 16)
                sp.dma_start(kstack[QAUX:QAUX + EXPERTS, slot, :, :].bitcast(F32),
                             rows_r[2 * EXPERTS:3 * EXPERTS, 0:SEQ].bitcast(F32).rearrange("p (o c) -> p o c", o=1)
                             .to_broadcast([EXPERTS, GH, SEQ])).then_inc(stack_dma[slot], 16)
                read(sp, j, ("Fp", g))
                for row, part in ((0, q_hi), (32, q_hi), (64, q_lo)):
                    for h in range(GH):
                        sp.dma_start(kstack[row:row + 32, slot, h, :].bitcast(F32),
                                     part[32 * h:32 * h + 32, 1, :].bitcast(F32)).then_inc(stack_dma[slot], 16)
                sp.wait_ge(qs_ready, 2 * (4 * j + g + 1))
                for row, part in ((0, qs_hi), (32, qs_lo), (64, qs_hi)):
                    for h in range(GH):
                        sp.dma_start(qstack[row:row + 32, slot, h, :].bitcast(F32),
                                     part[32 * h:32 * h + 32, :, :].bitcast(F32).rearrange("p a b -> p (a b)")
                                     ).then_inc(stack_dma[slot], 16)

            def max_row(j, g):
                read(sp, j, ("Fn", g))
                sp.dma_start(qstack[RMAXROW:RMAXROW + 1, g % RING, :, :].bitcast(F32), nmax_f[:, :].bitcast(F32)).then_inc(nmax_dma, 16)

            with sp.Fori(0, BATCH) as j:
                sp.wait_ge(x_copied, j)
                alone(sp)
                sp.wait_ge(xn_ready, 2 * j)
                alone(sp)
                sp.dma_start(xin[:], x[bass.ds(j, 1)].rearrange("o b t d -> t (o b) d")).then_inc(x_in, 16)
                sp.wait_ge(rows_r_ready, j + 1)
                stack(j, 0)
                stack(j, 1)
                max_row(j, 0)
                stack(j, 2)
                max_row(j, 1)
                stack(j, 3)
                max_row(j, 2)
                max_row(j, 3)

            sp.wait_ge(x2_dma, 16 * BATCH)
            sp.wait_ge(xt1_dma, 32 * BATCH)
            sp.dma_start(raw["ff1"], w_ff1).then_inc(loaded, 16)
            with sp.Fori(0, BATCH // 2) as t:
                sp.wait_ge(m_hid, FBLK * t)
                alone(sp)
                sp.dma_start(xm_hi[:].bitcast(F32), scratch_t2[bass.ds(t, 1), 0].rearrange("o b p c -> p (o b) c")).then_inc(m_in, 16)
                sp.dma_start(xm_lo[:].bitcast(F32), scratch_t2[bass.ds(t, 1), 1].rearrange("o b p c -> p (o b) c")).then_inc(m_in, 16)
                sp.wait_ge(m_x2, t)
                alone(sp)
                sp.dma_start(xm_res[:], scratch_x2[bass.ds(t, 1)].rearrange("o b p d -> p (o b) d")).then_inc(m_xin, 16)
                sp.wait_ge(m_out, t + 1)
                alone(sp)
                sp.dma_start(out2[bass.ds(t, 1)].rearrange("o b p d -> p (o b) d"), xm_out[:]).then_inc(out_dma, 16)
            sp.wait_ge(out_dma, 16 * (BATCH // 2))


        @block.tensor
        def _(pe):
            def split3(o, wname, cols, xi, xcols, weights_stationary, ready=None):
                hi, lo = W[wname]
                for n, (w, a) in enumerate(((hi, xt_hi), (hi, xt_lo), (lo, xt_hi))):
                    w_, a_ = w[:, cols], a[xi][:, xcols]
                    l, r = (w_, a_) if weights_stationary else (a_, w_)
                    mm = pe.matmul(o, l, r, start=(n == 0), stop=(n == 2))
                return mm

            def run(j, s):
                kind = s[0]
                if s in PROJ.where:
                    pe.wait_ge(proj_free[PROJ.bank(s)], PROJ.before(j, s))
                    o = proj(s)
                    done = proj_full[PROJ.bank(s)]
                if s in SCORES.where:
                    pe.wait_ge(sc_free[SCORES.bank(s)], SCORES.before(j, s))
                    o = scores(s)
                    done = sc_full[SCORES.bank(s)]
                if kind in ("T0", "T1"):
                    i = int(kind[1])
                    pe.wait_ge(xn_ready, 2 * j + i + 1)
                    for b in range(BLKS):
                        mm = pe.transpose(o[:, b * P:(b + 1) * P], xn[:, b, :], ident)
                    mm.then_inc(done, 1)
                elif kind == "RL":
                    read(pe, j, ("T0",))
                    for b in range(BLKS):
                        mm = split3(o[:, 4 * b:4 * b + 4], "rt", slice(0, 4), 0, slice(b * P, b * P + P), False)
                    mm.then_inc(done, 1)
                elif kind in ("Ap", "Cp"):
                    i = 0 if kind == "Ap" else 1
                    read(pe, j, ("T%d" % i,))
                    for t in range(2):
                        c = t * 1024 + s[1] * P
                        mm = split3(o[:, t * SEQ:(t + 1) * SEQ], "l%d" % i, slice(c, c + P), i, slice(0, SEQ), True)
                    mm.then_inc(done, 1)
                elif kind in ("Av", "Cv"):
                    i = 0 if kind == "Av" else 1
                    b, half = s[1] // 2, s[1] % 2
                    c = 2048 + 512 * half
                    split3(o, "l%d" % i, slice(c, c + 512), i, slice(b * P, b * P + P), False).then_inc(done, 1)
                elif kind == "RT":
                    pe.wait_ge(routes_ready, j + 1)
                    for c in range(2):
                        for b in range(BLKS):
                            k = (c * BLKS + b) * P
                            mm = pe.transpose(o[0:AUXC, k:k + P], routes[:, c, b, :], ident)
                    mm.then_inc(done, 1)
                elif kind in ("SB", "WB"):
                    a = CONST["expand"][0] + (P if kind == "WB" else 0)
                    read(pe, j, ("RT",))
                    pe.matmul(o, cst[0:AUXC, a:a + P], rows[:, :], start=True, stop=True).then_inc(done, 1)
                elif kind == "Am":
                    p = s[1]
                    read(pe, j, ("Ap", p))
                    for e in range(2):
                        r = slice(64 * e, 64 * e + 64)
                        q, k = qk_hi[r, p % NQK, 0, :], qk_hi[r, p % NQK, 1, :]
                        pe.matmul(o[:, e, 0:P], q[:, 0:P], k[:, 0:P], start=True, stop=True)
                        mm = pe.matmul(o[:, e, P:3 * P], q[:, P:2 * P], k[:, 0:SEQ], start=True, stop=True)
                    mm.then_inc(done, 1)
                elif kind == "An":
                    g = s[1]
                    read(pe, j, ("Am", 2 * g + 1))
                    for b in range(BLKS):
                        mm = pe.matmul(o[0:GH, b * P:(b + 1) * P], amax[:, b, GH * g:GH * g + GH], negident[:],
                                       start=True, stop=True)
                    mm.then_inc(done, 1)
                elif kind in ("As", "Cs"):
                    p = s[1]
                    if kind == "As":
                        read(pe, j, ("An", p // 2))
                    else:
                        read(pe, j, ("Cp", p))
                    passes = ((qk_hi, qk_hi), (qk_lo, qk_hi), (qk_hi, qk_lo))
                    for e in range(2):
                        r = slice(64 * e, 64 * e + 64)
                        for kb in range(BLKS):
                            oo = o[:, e, 0:SEQ] if kb == 0 else o[:, e, SEQ:SEQ + P]
                            for n, (k, q) in enumerate(passes):
                                mm = pe.matmul(oo, k[r, p % NQK, 1, kb * P:(kb + 1) * P],
                                               q[r, p % NQK, 0, kb * P:SEQ], start=(n == 0),
                                               stop=(n == 2 and kind == "Cs"))
                            if kind == "As":
                                mm = pe.matmul(oo, pick[:, (2 * p + e) % GH, :],
                                               nmax_a[:, kb * P:SEQ], start=False, stop=True)
                    mm.then_inc(done, 1)
                elif kind in ("Ao", "Co"):
                    p = s[1]
                    S = ("As" if kind == "Ao" else "Cs", p)
                    for half in (2, 3):
                        read(pe, j, ("Av" if kind == "Ao" else "Cv", half))
                    pe.wait_ge(mask_done, j * NMASK + MASKED[S] + 1)
                    pe.wait_ge(out_free[OUTS.bank(s)], OUTS.before(j, s))
                    o = outs(s)
                    pp = probs[:, PROBS.bank(S), 0:768].rearrange("p (c e q) -> p c e q", c=3, e=2)
                    for e in range(2):
                        h = 2 * p + e
                        for qb in range(BLKS):
                            oo = o[:, (2 * qb + e) * DHV:(2 * qb + e + 1) * DHV]
                            mm = pe.matmul(oo, pp[:, qb, e, :], v0[:, 0, h, :], start=True,
                                           stop=(qb == 0))
                            if qb:
                                mm = pe.matmul(oo, pp[:, 2, e, :], v0[:, 1, h, :], start=False, stop=True)
                    mm.then_inc(out_full[OUTS.bank(s)], 1)
                elif kind in ("At", "Ct"):
                    m = s[1]
                    read(pe, j, ("Co" if kind == "Ct" else "Ao", 2 * m))
                    read(pe, j, ("Co" if kind == "Ct" else "Ao", 2 * m + 1))
                    for pp in range(2):
                        for b in range(BLKS):
                            c = (2 * m + pp) * P
                            mm = pe.transpose(o[:, (2 * pp + b) * P:(2 * pp + b + 1) * P], an[:, b, c:c + P], ident)
                    mm.then_inc(done, 1)
                elif kind == "Fp":
                    g = s[1]
                    for t in range(2):
                        c = t * 512 + g * P
                        mm = split3(o[:, t * SEQ:(t + 1) * SEQ], "ffn", slice(c, c + P), 0, slice(0, SEQ), True)
                    mm.then_inc(done, 1)
                elif kind == "Fv":
                    b = s[1]
                    split3(o, "ffn", slice(1024, 1536), 0, slice(b * P, b * P + P), False).then_inc(done, 1)
                elif kind == "Fm":
                    g, h = s[1], s[2]
                    stacked(pe, j, g)
                    for c in range(SLOTS // P):
                        mm = pe.matmul(o[:, c // 2, (c % 2) * SEQ:(c % 2 + 1) * SEQ],
                                       qstack[0:RMAXROW, g % RING, h, c * P:(c + 1) * P],
                                       kstack[0:RMAXROW, g % RING, h, :], start=True, stop=True)
                    mm.then_inc(done, 1)
                elif kind == "Fn":
                    g = s[1]
                    read(pe, j, ("Fm", g, GH - 1))
                    for c in range(SLOTS // P):
                        mm = pe.matmul(o[0:GH, c * P:(c + 1) * P], rmax[:, c, GH * g:GH * g + GH], negident[:],
                                       start=True, stop=True)
                    mm.then_inc(done, 1)
                elif kind == "Fs":
                    g, h = s[1], s[2]
                    pe.wait_ge(nmax_dma, 16 * (4 * j + g + 1))
                    for kb in range(BLKS):
                        mm = pe.matmul(o[:, kb, :], kstack[0:RMAXROW + 1, g % RING, h, kb * P:(kb + 1) * P],
                                       qstack[0:RMAXROW + 1, g % RING, h, :], start=True, stop=True)
                    mm.then_inc(done, 1)
                elif kind == "Fo":
                    g, half = s[1], s[2]
                    read(pe, j, ("Fv", 1))
                    last = ("Fs", g, 2 * half + 1)
                    pe.wait_ge(sc_free[SCORES.bank(last)], SCORES.after(j, last))
                    if half == 0:
                        pe.wait_ge(out_free[0], OUTS.before(j, ("Fo", g)))
                        if g == 0:
                            pe.wait_ge(out_free[1], OUTS.before(j, ("Fsum",)))
                    a = CONST["sumcols"][0] + 32 * g
                    for kb in range(BLKS):
                        for h in (2 * half, 2 * half + 1):
                            pp = probs[:, PROBS.bank(("Fs", g, h)), kb * SLOTS:(kb + 1) * SLOTS]
                            c = (GH * g + h) * 32
                            mv_ = pe.matmul(ps[32 * h:32 * h + 32, 6, :], vf[:, kb, c:c + 32], pp,
                                            start=(kb == 0), stop=(kb == 1))
                            t = (h + 2) % 4
                            ms = pe.matmul(ps[32 * t:32 * t + 32, 7, :], cst[:, a:a + 32], pp,
                                           start=(kb == 0 and g == 0), stop=(kb == 1 and g == 3))
                            if kb == 1:
                                ms.then_inc(probs_used[PROBS.bank(("Fs", g, h))], 1)
                                if half and h == 2 * half + 1:
                                    mv_.then_inc(out_full[0], 1)
                                elif half and g == GROUPS - 1:
                                    mv_.then_inc(out_full[1], 1)
                    return
                elif kind == "Fe":
                    g = s[1]
                    read(pe, j, ("Fsum",))
                    a = CONST["spread"][0] + P * g
                    pe.matmul(o, cst[:, a:a + P], rsum[:, :], start=True, stop=True).then_inc(done, 1)
                elif kind in ("X1", "X2"):
                    i = int(kind[1]) - 1
                    for m in (2, 3):
                        read(pe, j, ("Ct" if i else "At", m))
                    if i == 0:
                        pe.wait_ge(y_ready, 4 * (j + 1))
                    for b in range(BLKS):
                        oo, tok = o[:, b * P:(b + 1) * P], slice(b * P, (b + 1) * P)
                        for m in range(8):
                            mm = pe.matmul(oo, at[:, m, tok], w_out[i][:, m, :], start=(m == 0),
                                           stop=(m == 7 and i == 1))
                        if i == 0:
                            for g in range(GROUPS):
                                pe.matmul(oo, y[:, g, tok], w_o[:, g, :], start=False, stop=False)
                            for c in range(2):
                                k = c * SEQ + b * P
                                mm = pe.matmul(oo, rows[:, k:k + P], b_o[:, :], start=False, stop=(c == 1))
                    mm.then_inc(done, 1)

            pe.wait_ge(w_lo, len(SPLIT))
            pe.wait_ge(consts_r, 2)
            pe.wait_ge(pool_c, 2)
            with pe.Fori(0, BATCH) as j:
                for s in ORDER:
                    run(j, s)

            pe.wait_ge(w_lo, len(SPLIT) + 1)
            with pe.Fori(0, BATCH // 2) as t:
                pe.wait_ge(m_in, 32 * (t + 1))
                for f in range(FBLK):
                    if f >= 2:
                        pe.wait_ge(m_pre, FBLK * t + f - 1)
                    else:
                        pe.wait_ge(m_pre, FBLK * t)
                    hi, lo = W["ff1"]
                    for n, (w, a) in enumerate(((hi, xm_hi), (hi, xm_lo), (lo, xm_hi))):
                        mm = pe.matmul(ps[:, f % 2, :], w[:, f * P:(f + 1) * P], a[:].rearrange("p b c -> p (b c)"),
                                       start=(n == 0), stop=(n == 2))
                    mm.then_inc(m_hid, 1)
                pe.wait_ge(m_act, FBLK * (t + 1))
                pe.wait_ge(m_out, t)
                for c in range(4):
                    for f in range(FBLK):
                        mm = pe.matmul(ps[:, 2, c * P:(c + 1) * P], act_t[:, f, c * P:(c + 1) * P], w_2[:, f, :],
                                       start=(f == 0), stop=(f == FBLK - 1))
                mm.then_inc(m_sum, 1)

        @block.scalar
        def _(act):
            actn = [0]

            def run(j, s):
                kind = s[0]
                if kind in ("T0", "T1"):
                    i = int(kind[1])
                    full(act, j, s)
                    if i:
                        act.wait_ge(xt1_dma, 32 * j)
                    nc.scalar.activation(xt_hi[i], proj(s)[:, 0:SEQ], ACT.Copy).then_inc(xt_hi_s, 1)
                    if i:
                        read(act, j, ("T1",))
                        act.dma_start(scratch_t[bass.ds(j, 1), 0].rearrange("o p c -> p (o c)"), xt_hi[1].bitcast(F32)
                                      ).then_inc(xt1_dma, 16)
                        act.dma_start(scratch_t[bass.ds(j, 1), 1].rearrange("o p c -> p (o c)"), xt_lo[1].bitcast(F32)
                                      ).then_inc(xt1_dma, 16)
                elif kind in ("Ap", "Cp"):
                    if s == ("Ap", 1):
                        read(act, j, ("RL",))
                        nc.scalar.activation(ex[:], lg[:], ACT.Exp).then_inc(ex_ready, 1)
                    p = s[1]
                    full(act, j, s)
                    if kind == "Ap":
                        for t in range(2):
                            mm = nc.scalar.activation(qk_hi[:, p % NQK, t, :], proj(s)[:, t * SEQ:(t + 1) * SEQ],
                                                      ACT.Identity, bias=b_qk0[:, 8 * t + p:8 * t + p + 1])
                    else:
                        mm = nc.scalar.activation(qk_hi[:, p % NQK, :, :].rearrange("p a b -> p (a b)"), proj(s),
                                                  ACT.Copy)
                    mm.then_inc(a_hi, 1)
                elif kind == "Cv":
                    b, half = s[1] // 2, s[1] % 2
                    full(act, j, s)
                    nc.scalar.activation(v0[:, b, 8 * half:8 * half + 8, 0:DH],
                                         proj(s).rearrange("p (h d) -> p h d", h=8), ACT.Copy).then_inc(freed(s), 1)
                elif kind == "RT":
                    read(act, j, ("RT",))
                    nc.scalar.activation(rows_r[:], rows[:], ACT.Copy).then_inc(rows_r_ready, 1)
                elif kind == "SB":
                    full(act, j, s)
                    nc.scalar.activation(sel_bc[:].rearrange("p a b -> p (a b)"), proj(s), ACT.Copy
                                         ).then_inc(freed(s), 1)
                elif kind == "WB":
                    full(act, j, s)
                    nc.scalar.activation(w_bc[:], proj(s), ACT.Copy).then_inc(freed(s), 1)
                elif kind == "An":
                    full(act, j, s)
                    nc.scalar.activation(nmax_a[:], proj(s)[0:GH, 0:SEQ], ACT.Copy
                                         ).then_inc(freed(s), 1)
                elif kind in ("As", "Cs"):
                    buffer_used(j, s)
                    full(act, j, s)
                    flat = probs[:, PROBS.bank(s), 0:768]
                    pp = flat.rearrange("p (c e q) -> p e c q", c=3, e=2)
                    sc = scores(s)[:, :, 0:384].rearrange("p e (c q) -> p e c q", c=3)
                    if kind == "As":
                        nc.scalar.activation(pp, sc, ACT.Exp, scale=L0_SCALE
                                             ).then_inc(freed(s), 1)
                    else:
                        nc.scalar.activation(pp, sc, ACT.Tanh, scale=L0_SCALE / CLAMP
                                             ).then_inc(freed(s), 1)
                        full_read(j, s)
                        nc.scalar.activation(flat, flat, ACT.Exp, scale=CLAMP).then_inc(c_exp, 1)
                elif kind in ("At", "Ct"):
                    full(act, j, s)
                    m = s[1]
                    nc.scalar.activation(at[:, 2 * m:2 * m + 2, :].rearrange("p a b -> p (a b)"), proj(s), ACT.Copy
                                         ).then_inc(freed(s), 1)
                elif kind == "Fp":
                    g = s[1]
                    full(act, j, s)
                    stacked(act, j, g - 1)
                    for t in range(2):
                        mm = nc.scalar.activation(q_hi[:, t, :], proj(s)[:, t * SEQ:(t + 1) * SEQ], ACT.Identity,
                                                  bias=b_qkf[:, 4 * t + g:4 * t + g + 1])
                    mm.then_inc(f_hi, 1)
                elif kind == "Fn":
                    full(act, j, s)
                    nc.scalar.activation(nmax_f[:], proj(s)[0:GH, :], ACT.Copy).then_inc(freed(s), 1)
                elif kind == "Fs":
                    buffer_used(j, s)
                    full(act, j, s)
                    nc.scalar.activation(probs[:, PROBS.bank(s), :], scores(s).rearrange("p a b -> p (a b)"),
                                         ACT.Exp, scale=ROUTED_SCALE).then_inc(freed(s), 1)
                elif kind == "X2":
                    read(act, j, ("X2",))
                    act.dma_start(scratch_x[bass.ds(j, 1)].rearrange("o b p d -> p (o b) d"), x2[:]).then_inc(x2_dma, 16)

            def buffer_used(j, s):
                n = EXPS[s]
                if n < 4:
                    for b in (0, 1):
                        act.wait_ge(out_full[b], j * OUTS.n[b])
                else:
                    last = exp_order()[n - 4]
                    if last[0] == "Fs":
                        act.wait_ge(probs_used[n % 4], 4 * j + (n - 4 - PAIRS) // 4 + 1)
                    else:
                        full(act, j, (last[0][0] + "o", last[1]))

            def full_read(j, s):
                act.wait_ge(sc_free[SCORES.bank(s)], SCORES.after(j, s))

            act.wait_ge(loaded, 16 * NLOAD)
            for name in SPLIT:
                nc.scalar.activation(W[name][0][:], raw[name], ACT.Copy).then_inc(w_hi, 1)
            nc.scalar.activation(negident[:], raw["cst"][:, GH * P:GH * P + P], ACT.Copy).then_inc(consts_r, 1)
            nc.scalar.activation(pick[:].rearrange("p a b -> p (a b)"), raw["cst"][0:GH, 0:GH * P], ACT.Copy
                                 ).then_inc(consts_r, 1)
            act.wait_ge(th_ready, 1)
            nc.scalar.activation(sc_th[:, 0, :], th[:, 0, :], ACT.Sin)
            nc.scalar.activation(sc_th[:, 1, :], th[:, 1, :], ACT.Sin).then_inc(sc_ready, 1)
            with act.Fori(0, BATCH) as j:
                for s in ORDER:
                    run(j, s)

            act.wait_ge(loaded, 16 * (NLOAD + 1))
            nc.scalar.activation(W["ff1"][0], raw["ff1"], ACT.Copy).then_inc(w_hi, 1)
            act.wait_ge(amp_ready, 1)
            with act.Fori(0, BATCH // 2) as t:
                for f in range(FBLK):
                    act.wait_ge(m_hid, FBLK * t + f + 1)
                    if f >= 2:
                        act.wait_ge(m_frac, FBLK * t + f - 1)
                    else:
                        act.wait_ge(m_frac, FBLK * t)
                    nc.scalar.activation(turns[:, f % 2, :], ps[:, f % 2, :], ACT.Identity, scale=0.1 / (2 * PI),
                                         bias=amp[:, 1, f:f + 1]).then_inc(m_turns, 1)
                    act.wait_ge(m_frac, FBLK * t + f + 1)
                    nc.scalar.activation(sine[:, f % 2, :], frac[:, f % 2, :], ACT.Sin, scale=6.283185).then_inc(m_sine, 1)
                    act.wait_ge(m_pre, FBLK * t + f + 1)
                    if f == 0:
                        act.wait_ge(m_sum, t)
                    nc.scalar.activation(act_t[:, f, :], pre[:, f % 2, :], ACT.Relu, bias=fc[:, 3, f:f + 1]
                                         ).then_inc(m_act, 1)

        @block.gpsimd
        def _(pool):
            def run(j, s):
                kind = s[0]
                if kind in ("T0", "X1"):
                    pool.wait_ge(var_ready, 2 * j + int(kind == "X1") + 1)
                    nc.gpsimd.tensor_tensor(rstd[:], ve[:], neghalf[:], ALU.pow).then_inc(rstd_ready, 1)
                if kind == "T0":
                    pool.wait_ge(x_in, 16 * (j + 1))
                    pool.wait_ge(proj_free[PROJ.bank(("X1",))], PROJ.n[PROJ.bank(("X1",))] * j)
                    nc.gpsimd.tensor_tensor(xres[:], xin[:], b_out[:].rearrange("p (o d) -> p o d", o=1)
                                            .to_broadcast([P, BLKS, D]), ALU.add).then_inc(x_copied, 1)
                elif kind in ("As", "Cs"):
                    if kind == "As":
                        read(pool, j, s)
                    else:
                        pool.wait_ge(c_exp, PAIRS * j + s[1] + 1)
                    alone(pool)
                    pp = probs[:, PROBS.bank(s), 0:768].rearrange("p (c r) -> p c r", c=3)[:, 0:3:2, :]
                    nc.gpsimd.affine_select(out=pp, in_=pp, compare_op=ALU.is_ge, fill=0.0, base=0,
                                            pattern=[[0, 2], [0, 2], [1, P]], channel_multiplier=-1
                                            ).then_inc(mask_done, 1)
                elif kind == "Fp":
                    g = s[1]
                    read(pool, j, ("Fp", g))
                    stacked(pool, j, g - 1)
                    if g == 0:
                        read(pool, j, ("SB",))
                    for dst, src in ((qs_hi, q_hi), (qs_lo, q_lo)):
                        nc.gpsimd.tensor_tensor(dst[:], src[:, 0:1, :].to_broadcast([P, 2, SEQ]), sel_bc[:], ALU.mult
                                                ).then_inc(qs_ready, 1)
                elif kind == "Fe":
                    g = s[1]
                    read(pool, j, s)
                    nc.gpsimd.tensor_tensor(y[:, g, :], y2[:, g % 2, 0, :], y2[:, g % 2, 1, :], ALU.add
                                            ).then_inc(y_ready, 1)

            nc.gpsimd.memset(v0[:, :, :, DH:DHV], 1.0).then_inc(pool_c, 1)
            nc.gpsimd.memset(neghalf[:], -0.5).then_inc(pool_c, 1)
            pool.wait_ge(pool_c, 2)
            with pool.Fori(0, BATCH) as j:
                for s in ORDER:
                    run(j, s)
            with pool.Fori(0, BATCH // 2) as t:
                pool.wait_ge(m_xin, 16 * (t + 1))
                pool.wait_ge(m_out, t)
                nc.gpsimd.tensor_tensor(xm_resb[:], xm_res[:], b_2[:].rearrange("p (o d) -> p o d", o=1)
                                        .to_broadcast([P, 4, D]), ALU.add).then_inc(m_x2, 1)

        @block.vector
        def _(dve):
            n_chain = {"loop": 0, "pre": 0}
            where = ["pre"]
            LOOP_CHAIN = 30

            def link(ins, j=None):
                ins.then_inc(dve_c, 1)
                n_chain[where[0]] += 1
                k = n_chain["pre"]
                if j is not None:
                    k = j * LOOP_CHAIN + (k + n_chain["loop"])
                dve.wait_ge(dve_c, k)

            def norm(j, src, i):
                for b in range(BLKS):
                    ins = nc.vector.bn_stats(st[:, b, :], src[:, b, :])
                link(ins, j)
                alone(dve)
                for b in range(BLKS):
                    ins = nc.vector.bn_aggr(mv[:, b, :], st[:, b, :])
                link(ins, j)
                nc.vector.tensor_scalar(ve[:], mv[:, :, 1], EPS, None, ALU.add).then_inc(var_ready, 1)
                dve.wait_ge(rstd_ready, 2 * j + i + 1)
                for b in range(BLKS):
                    ins = nc.vector.tensor_scalar(xn[:, b, :], src[:, b, :], mv[:, b, 0:1], rstd[:, b:b + 1],
                                                  ALU.subtract, ALU.mult)
                ins.then_inc(xn_ready, 1)

            def lead(j, s):
                if s == ("T0",):
                    dve.wait_ge(x_in, 16 * (j + 1))
                    norm(j, xin, 0)
                elif s == ("Av", 0):
                    dve.wait_ge(ex_ready, j + 1)
                    link(nc.vector.tensor_reduce(r1[:], ex[:], AX.X, ALU.add), j)
                    link(nc.vector.reciprocal(r2[:], r1[:]), j)
                    link(nc.vector.tensor_tensor(pr[:], ex[:], r2[:].rearrange("p (b o) -> p b o", o=1)
                                                 .to_broadcast([P, BLKS, EXPERTS]), ALU.mult), j)
                    for b in range(BLKS):
                        mine = pr[:, b, :].rearrange("p (e o) -> p e o", o=1).to_broadcast([P, EXPERTS, EXPERTS])
                        other = pr[:, b, :].rearrange("p (o e) -> p o e", o=1).to_broadcast([P, EXPERTS, EXPERTS])
                        nc.vector.tensor_tensor(cmp1[:, b, :, :], mine, other, ALU.is_lt)
                        ins = nc.vector.tensor_tensor(cmp2[:, b, :, :], mine, other, ALU.is_equal)
                    link(ins, j)
                    link(nc.vector.tensor_tensor(cmp2[:].rearrange("p b e o -> p (b e o)"),
                                                 cmp2[:].rearrange("p b e o -> p (b e o)"), const("tie"), ALU.mult), j)
                    link(nc.vector.tensor_tensor(cmp1[:].rearrange("p b e o -> p (b e o)"),
                                                 cmp1[:].rearrange("p b e o -> p (b e o)"),
                                                 cmp2[:].rearrange("p b e o -> p (b e o)"), ALU.add), j)
                    link(nc.vector.tensor_reduce(rank[:], cmp1[:], AX.X, ALU.add), j)
                    for c in range(2):
                        nc.vector.tensor_scalar(routes[:, c, :, 0:4], rank[:], float(c), None, ALU.is_equal)
                        ins = nc.vector.tensor_scalar(routes[:, c, :, 8:12], rank[:], 2.0, None, ALU.is_lt)
                    link(ins, j)
                    for c in range(2):
                        nc.vector.tensor_tensor(routes[:, c, :, 4:8], routes[:, c, :, 0:4], pr[:], ALU.mult)
                        ins = nc.vector.tensor_scalar(routes[:, c, :, 8:12], routes[:, c, :, 8:12], 1.0, FAR,
                                                      ALU.subtract, ALU.mult)
                    ins.then_inc(routes_ready, 1)

            def run(j, s):
                kind = s[0]
                lead(j, s)
                if kind in ("T0", "T1"):
                    i = int(kind[1])
                    full(dve, j, s)
                    dve.wait_ge(xt_hi_s, 2 * j + i + 1)
                    if i:
                        dve.wait_ge(xt1_dma, 32 * j)
                    ins = nc.vector.tensor_tensor(xt_lo[i], proj(s)[:, 0:SEQ], xt_hi[i], ALU.subtract)
                    ins.then_inc(freed(s), 1)
                elif kind == "RL":
                    full(dve, j, s)
                    link(nc.vector.tensor_tensor(lg[:].rearrange("p b e -> p (b e)"), proj(s)[:, 0:BLKS * EXPERTS],
                                                 b_rt[:], ALU.add), j)
                    link(nc.vector.tensor_reduce(r3[:], lg[:], AX.X, ALU.max), j)
                    nc.vector.tensor_tensor(lg[:], lg[:], r3[:].rearrange("p (b o) -> p b o", o=1)
                                            .to_broadcast([P, BLKS, EXPERTS]), ALU.subtract).then_inc(freed(s), 1)
                elif kind in ("Ap", "Cp"):
                    p = s[1]
                    full(dve, j, s)
                    dve.wait_ge(a_hi, 16 * j + (PAIRS if kind == "Cp" else 0) + p + 1)
                    if kind == "Ap":
                        for t in range(2):
                            ins = nc.vector.scalar_tensor_tensor(
                                out=qk_lo[:, p % NQK, t, :], in0=proj(s)[:, t * SEQ:(t + 1) * SEQ],
                                scalar=b_qk0[:, 8 * t + p:8 * t + p + 1], in1=qk_hi[:, p % NQK, t, :],
                                op0=ALU.add, op1=ALU.subtract)
                    else:
                        ins = nc.vector.tensor_tensor(qk_lo[:, p % NQK, :, :].rearrange("p a b -> p (a b)"), proj(s),
                                                      qk_hi[:, p % NQK, :, :].rearrange("p a b -> p (a b)"),
                                                      ALU.subtract)
                    ins.then_inc(freed(s), 1)
                elif kind == "Av":
                    b, half = s[1] // 2, s[1] % 2
                    full(dve, j, s)
                    nc.vector.tensor_tensor(v0[:, b, 8 * half:8 * half + 8, 0:DH],
                                            proj(s).rearrange("p (h d) -> p h d", h=8),
                                            b_v0[:, 8 * half:8 * half + 8, :], ALU.add).then_inc(freed(s), 1)
                elif kind == "RT":
                    full(dve, j, s)
                    nc.vector.tensor_copy(rows[:], proj(s)[0:AUXC, :]).then_inc(freed(s), 1)
                elif kind == "Am":
                    p = s[1]
                    full(dve, j, s)
                    nc.vector.tensor_reduce(amax[:, 0, 2 * p:2 * p + 2], scores(s)[:, :, 0:P], AX.X, ALU.max)
                    nc.vector.tensor_reduce(amax[:, 1, 2 * p:2 * p + 2], scores(s)[:, :, P:3 * P], AX.X, ALU.max
                                            ).then_inc(freed(s), 1)
                elif kind in ("Ao", "Co"):
                    p = s[1]
                    full(dve, j, s)
                    o = outs(s)[:, 0:4 * DHV].rearrange("p (a c) -> p a c", c=DHV)
                    link(nc.vector.reciprocal(ra[:, p % 2, :].rearrange("p (a o) -> p a o", o=1), o[:, :, DH:DHV]), j)
                    for b in range(BLKS):
                        ins = nc.vector.tensor_tensor(
                            an[:, b, 2 * p * DH:(2 * p + 2) * DH].rearrange("p (e d) -> p e d", e=2),
                            o[:, 2 * b:2 * b + 2, 0:DH],
                            ra[:, p % 2, 2 * b:2 * b + 2].rearrange("p (e o) -> p e o", o=1)
                            .to_broadcast([P, 2, DH]), ALU.mult)
                    ins.then_inc(freed(s), 1)
                elif kind == "Fp":
                    g = s[1]
                    full(dve, j, s)
                    dve.wait_ge(f_hi, 4 * j + g + 1)
                    dve.wait_ge(qs_ready, 2 * (4 * j + g))
                    for t in range(2):
                        ins = nc.vector.scalar_tensor_tensor(
                            out=q_lo[:, t, :], in0=proj(s)[:, t * SEQ:(t + 1) * SEQ],
                            scalar=b_qkf[:, 4 * t + g:4 * t + g + 1], in1=q_hi[:, t, :], op0=ALU.add,
                            op1=ALU.subtract)
                    ins.then_inc(freed(s), 1)
                elif kind == "Fv":
                    full(dve, j, s)
                    nc.vector.tensor_tensor(vf[:, s[1], :], proj(s), b_vf[:], ALU.add).then_inc(freed(s), 1)
                elif kind == "Fm":
                    h = GH * s[1] + s[2]
                    full(dve, j, s)
                    nc.vector.tensor_reduce(rmax[:, :, h:h + 1].rearrange("p c o -> p (c o)"),
                                            scores(s).rearrange("p a (b c) -> p (a b) c", b=2), AX.X, ALU.max
                                            ).then_inc(freed(s), 1)
                elif kind == "Fo" and s[2] == 1:
                    g = s[1]
                    full(dve, j, ("Fo", g))
                    ins = nc.vector.tensor_tensor(u[:, g, :], ps[:, 6, :], w_bc[:], ALU.mult)
                    ins.then_inc(out_free[0], 1)
                    if g == GROUPS - 1:
                        dve.wait_ge(probs_used[PROBS.bank(("Fs", g, GH - 1))], 4 * (j + 1))
                        read(dve, j, ("Fo", g))
                        nc.vector.reciprocal(rsum[:], ps[:, 7, :]).then_inc(out_free[1], 1)
                elif kind == "Fe":
                    g = s[1]
                    full(dve, j, s)
                    if g >= 2:
                        dve.wait_ge(y_ready, 4 * j + g - 1)
                    nc.vector.tensor_tensor(y2[:, g % 2, :, :].rearrange("p a b -> p (a b)"), proj(s), u[:, g, :],
                                            ALU.mult).then_inc(freed(s), 1)
                elif kind == "X1":
                    full(dve, j, s)
                    nc.vector.tensor_tensor(x1[:].rearrange("p b d -> p (b d)"), proj(s)[:, 0:BLKS * D],
                                            xres[:].rearrange("p b d -> p (b d)"), ALU.add).then_inc(freed(s), 1)
                    read(dve, j, ("X1",))
                    norm(j, x1, 1)
                elif kind == "X2":
                    full(dve, j, s)
                    dve.wait_ge(x2_dma, 16 * j)
                    nc.vector.tensor_tensor(x2[:].rearrange("p b d -> p (b d)"), proj(s)[:, 0:BLKS * D],
                                            x1[:].rearrange("p b d -> p (b d)"), ALU.add).then_inc(freed(s), 1)

            dve.wait_ge(loaded, 16 * NLOAD)
            for n, name in enumerate(SPLIT):
                dve.wait_ge(w_hi, n + 1)
                nc.vector.tensor_tensor(W[name][1][:], raw[name], W[name][0][:], ALU.subtract).then_inc(w_lo, 1)
            dve.wait_ge(w_lo, len(SPLIT))
            nc.vector.memset(kstack[QAUX:P, :, :, :].rearrange("p a b c -> p (a b c)").bitcast(F32), 1.0).then_inc(ones_set, 1)

            theta, wr, wi, b1 = (fc[:, i, :] for i in range(4))
            link(nc.vector.tensor_scalar(tmp[:, 0, :], theta, 1 / (2 * PI), MAGIC, ALU.mult, ALU.add))
            link(nc.vector.tensor_scalar(tmp[:, 0, :], tmp[:, 0, :], MAGIC, None, ALU.subtract))
            src = theta
            for n, c in enumerate(TWO_PI_PARTS):
                link(nc.vector.scalar_tensor_tensor(out=tmp[:, 1 + n, :], in0=tmp[:, 0, :], scalar=-c, in1=src,
                                                    op0=ALU.mult, op1=ALU.add))
                src = tmp[:, 1 + n, :]
            link(nc.vector.tensor_scalar(th[:, 0, :], src, -3.1415925, 3.1415925, ALU.max, ALU.min))
            link(nc.vector.scalar_tensor_tensor(out=th[:, 1, :], in0=th[:, 0, :], scalar=-1.0, in1=th[:, 0, :],
                                                op0=ALU.mult, op1=ALU.max))
            nc.vector.tensor_scalar(th[:, 1, :], th[:, 1, :], -1.0, PI / 2, ALU.mult, ALU.add).then_inc(th_ready, 1)
            link(nc.vector.scalar_tensor_tensor(out=tmp[:, 0, :], in0=b1, scalar=0.1, in1=src, op0=ALU.mult,
                                                op1=ALU.add))
            link(nc.vector.tensor_scalar(amp[:, 1, :], tmp[:, 0, :], 1 / (2 * PI), None, ALU.mult))

            dve.wait_ge(sc_ready, 1)
            nc.vector.tensor_tensor(tmp[:, 0, :], sc_th[:, 1, :], wr, ALU.mult)
            nc.vector.tensor_tensor(tmp[:, 1, :], sc_th[:, 0, :], wi, ALU.mult).then_inc(amp_c, 1)
            dve.wait_ge(amp_c, 1)
            nc.vector.tensor_tensor(tmp[:, 2, :], tmp[:, 0, :], tmp[:, 1, :], ALU.add).then_inc(amp_c, 1)
            dve.wait_ge(amp_c, 2)
            nc.vector.scalar_tensor_tensor(out=amp[:, 0, :], in0=tmp[:, 2, :], scalar=0.1, in1=wi, op0=ALU.mult,
                                           op1=ALU.mult).then_inc(amp_ready, 1)
            where[0] = "loop"
            with dve.Fori(0, BATCH) as j:
                for s in ORDER:
                    run(j, s)
            assert n_chain["loop"] == LOOP_CHAIN, n_chain

            dve.wait_ge(w_hi, len(SPLIT) + 1)
            nc.vector.tensor_tensor(W["ff1"][1], raw["ff1"], W["ff1"][0], ALU.subtract).then_inc(w_lo, 1)
            with dve.Fori(0, BATCH // 2) as t:
                for f in range(FBLK):
                    n = FBLK * t + f + 1
                    dve.wait_ge(m_turns, n)
                    nc.vector.tensor_scalar(whole[:, f % 2, :], turns[:, f % 2, :], MAGIC, MAGIC, ALU.add,
                                            ALU.subtract).then_inc(m_whole, 1)
                    dve.wait_ge(m_whole, n)
                    nc.vector.tensor_tensor(frac[:, f % 2, :], turns[:, f % 2, :], whole[:, f % 2, :], ALU.subtract
                                            ).then_inc(m_frac, 1)
                    dve.wait_ge(m_sine, n)
                    nc.vector.scalar_tensor_tensor(out=pre[:, f % 2, :], in0=sine[:, f % 2, :],
                                                   scalar=amp[:, 0, f:f + 1], in1=ps[:, f % 2, :], op0=ALU.mult,
                                                   op1=ALU.add).then_inc(m_pre, 1)
                dve.wait_ge(m_sum, t + 1)
                dve.wait_ge(m_x2, t + 1)
                dve.wait_ge(out_dma, 16 * t)
                nc.vector.tensor_tensor(xm_out[:].rearrange("p b d -> p (b d)"), ps[:, 2, :],
                                        xm_resb[:].rearrange("p b d -> p (b d)"), ALU.add).then_inc(m_out, 1)


def constants():
    import numpy as np

    c = {n: np.zeros((P, w), np.float32) for n, (_, w) in CONST.items()}
    c["ident"][:] = np.eye(P)
    c["negident"][:] = -np.eye(P)
    for g in range(GROUPS):
        for h in range(GH):
            c["spread"][32 * ((h + 2) % 4) + g, P * g + 32 * h:P * g + 32 * h + 32] = 1
            c["pick"][h, P * h:P * h + P] = 1
        c["sumcols"][:, 32 * g + g:32 * g + 32:4] = 1
    for e in range(EXPERTS):
        for h in range(GH):
            r = 32 * h + HE * e
            c["expand"][e, r:r + HE] = 1
            c["expand"][EXPERTS + e, P + r:P + r + HE] = 1
    tie = np.array([[float(o < e) for o in range(EXPERTS)] for e in range(EXPERTS)], np.float32)
    c["tie"][:] = np.tile(tie.ravel(), BLKS)
    return np.concatenate([c[n] for n in CONST], axis=1)


def kernel(**inputs):
    import numpy as np
    import concourse.bacc as bacc
    from concourse.bass_utils import run_bass_kernel_spmd

    i = {k: np.asarray(v) for k, v in inputs.items()}
    qkv = i["L0_attn_qkv_w"].reshape(D, HEADS, 3, DH)
    qkv_b = i["L0_attn_qkv_b"].reshape(HEADS, 3, DH)

    def rowsof(v):
        return np.broadcast_to(v.reshape(1, -1), (P, v.size))

    def experts_in(w):
        return w.reshape(EXPERTS, D, HEADS, HE).transpose(1, 2, 0, 3).reshape(D, HEADS * EXPERTS * HE)

    def experts_b(b):
        return b.reshape(EXPERTS, HEADS, HE).transpose(1, 0, 2).reshape(-1)

    bo = np.zeros((AUXC, D), np.float32)
    bo[EXPERTS:2 * EXPERTS] = i["L0_ffn_bo"]
    arrays = {
        "x": i["L0_attn_x"].reshape(BATCH, BLKS, P, D),
        "w_l0": qkv.transpose(0, 2, 1, 3).reshape(D, 3 * HEADS * DH),
        "w_l1": np.concatenate([i["L1_attn_W" + n].T for n in "qkv"], axis=1),
        "w_ffn": np.concatenate([experts_in(i["L0_ffn_w" + n]) for n in "qkv"], axis=1),
        "w_ff1": i["L1_ffn_W1"],
        "router_w": i["L0_ffn_router_w"],
        "out_w0": i["L0_attn_out_w"].reshape(8, P, D).transpose(1, 0, 2),
        "out_w1": i["L1_attn_Wo"].T.reshape(8, P, D).transpose(1, 0, 2),
        "wo": i["L0_ffn_wo"].reshape(EXPERTS, GROUPS, GH, HE, D).transpose(2, 0, 3, 1, 4).reshape(P, GROUPS, D),
        "w_ff2": i["L1_ffn_W2"].reshape(FBLK, P, D).transpose(1, 0, 2),
        "bias_qk0": np.concatenate([qkv_b[:, n].reshape(PAIRS, P).T for n in (0, 1)], axis=1),
        "bias_v0": rowsof(qkv_b[:, 2]),
        "bias_qkf": np.concatenate([experts_b(i["L0_ffn_b" + n]).reshape(GROUPS, P).T for n in "qk"], axis=1),
        "bias_vf": rowsof(experts_b(i["L0_ffn_bv"])),
        "router_b": rowsof(np.concatenate([i["L0_ffn_router_b"]] * BLKS)),
        "out_b": rowsof(i["L0_attn_out_b"]),
        "bo": bo,
        "ff_cols": np.stack([i["L1_ffn_" + n].reshape(FBLK, P).T for n in (
            "quantum_phases", "quantum_weights_real", "quantum_weights_imag", "b1")], axis=1),
        "ff_b2": rowsof(i["L1_ffn_b2"]),
        "consts": constants(),
    }
    nc = bacc.Bacc("TRN2", target_bir_lowering=False, num_devices=1)
    args, feeds = [], {}
    for name, a in arrays.items():
        a = np.ascontiguousarray(a)
        feeds["in_" + name] = a
        args.append(nc.dram_tensor("in_" + name, a.shape, mybir.dt.from_np(a.dtype), kind="ExternalInput").ap())
    args.append(nc.dram_tensor("scratch_x", (BATCH, BLKS, P, D), F32).ap())
    args.append(nc.dram_tensor("scratch_t", (BATCH, 2, P, SEQ), F32).ap())
    args.append(nc.dram_tensor("out_0", (BATCH, BLKS, P, D), F32, kind="ExternalOutput").ap())
    blocks(nc, *args)
    r = run_bass_kernel_spmd(nc, [feeds], core_ids=[0])
    return r.results[0]["out_0"].reshape(BATCH, SEQ, D)
```
